# Optimizing a Trainium2 kernel written in Bass

```python
import numpy as np
import jax
import jax.numpy as jnp

def _softmax(x, axis=-1):
    return jax.nn.softmax(x, axis=axis)

def _gelu(x):
    return jax.nn.gelu(x, approximate=True)

def _silu(x):
    return jax.nn.silu(x)

def _sigmoid(x):
    return jax.nn.sigmoid(x)

def _layernorm(x, axis=-1, eps=1e-05):
    m = jnp.mean(x, axis=axis, keepdims=True)
    v = jnp.var(x, axis=axis, keepdims=True)
    return (x - m) / jnp.sqrt(v + eps)

def _scatter_add(tgt, idx, src, axis=0):
    return tgt.at[idx].add(src)

def _segment_sum(src, seg, n):
    return jax.ops.segment_sum(src, seg, n)
kernel_name = 'mk_adj_preln_d1_adj_r2_3db841'

def setup_inputs(seed: int=0):
    np.random.seed(seed)
    _w = jnp.asarray

    def _rec_inputs():
        import jax
        import jax.numpy as jnp
        _gk = jax.random.key(seed)
        x = -0.001547 + 1.001 * jax.random.normal(jax.random.fold_in(_gk, 1), (512, 128), jnp.float32)
        _a = jax.random.bernoulli(jax.random.fold_in(_gk, 2), 0.00390625, (512, 512))
        _a = jnp.logical_or(_a, jnp.swapaxes(_a, -1, -2))
        _a = jnp.logical_or(_a, jnp.eye(512, dtype=bool))
        adj = _a.astype(jnp.int32)
        return (x, adj)
    x, adj = _rec_inputs()

    def _L0_gnn_setup():
        import jax, jax.numpy as jnp
        import numpy as np
        BT, BN, D, H = (512, 512, 128, 8)
        DH = D // H
        key = jax.random.key(seed)
        ks = jax.random.split(key, 16)
        s = 1.0 / np.sqrt(D)
        return {'h_target': jax.random.normal(ks[0], (BT, D), jnp.float32), 'h_neigh': jax.random.normal(ks[1], (BN, D), jnp.float32), 'adjacency': jax.random.randint(ks[2], (BT, BN), 0, 2, jnp.int32), 'edge_types': jax.random.randint(ks[3], (BT, BN), 0, 2, jnp.int32), 'Wq': jax.random.normal(ks[4], (D, D), jnp.float32) * s, 'bq': jnp.zeros((D,), jnp.float32), 'Wk': jax.random.normal(ks[5], (D, D), jnp.float32) * s, 'bk': jnp.zeros((D,), jnp.float32), 'Wv': jax.random.normal(ks[6], (D, D), jnp.float32) * s, 'bv': jnp.zeros((D,), jnp.float32), 'Wo': jax.random.normal(ks[7], (D, D), jnp.float32) * s, 'bo': jnp.zeros((D,), jnp.float32), 'E': jax.random.normal(ks[8], (2, D), jnp.float32)}
    _L0_gnn_all = _L0_gnn_setup()
    _L0_gnn_in = {k: v for k, v in _L0_gnn_all.items() if k in ('h_neigh', 'Wq', 'bq', 'Wk', 'bk', 'Wv', 'bv', 'Wo', 'bo', 'E')}
    del _L0_gnn_all
    return {'x': x, 'adj': adj, 'L0_gnn_h_neigh': _L0_gnn_in['h_neigh'], 'L0_gnn_Wq': _L0_gnn_in['Wq'], 'L0_gnn_bq': _L0_gnn_in['bq'], 'L0_gnn_Wk': _L0_gnn_in['Wk'], 'L0_gnn_bk': _L0_gnn_in['bk'], 'L0_gnn_Wv': _L0_gnn_in['Wv'], 'L0_gnn_bv': _L0_gnn_in['bv'], 'L0_gnn_Wo': _L0_gnn_in['Wo'], 'L0_gnn_bo': _L0_gnn_in['bo'], 'L0_gnn_E': _L0_gnn_in['E']}

def reference(x, adj, L0_gnn_h_neigh, L0_gnn_Wq, L0_gnn_bq, L0_gnn_Wk, L0_gnn_bk, L0_gnn_Wv, L0_gnn_bv, L0_gnn_Wo, L0_gnn_bo, L0_gnn_E):
    import jax
    import jax.numpy as jnp

    def _L0_gnn_ref(h_target, h_neigh, adjacency, edge_types, Wq, bq, Wk, bk, Wv, bv, Wo, bo, E):
        import jax, jax.numpy as jnp
        import numpy as np
        BT, BN, D, H = (512, 512, 128, 8)
        DH = D // H
        Bt, d = h_target.shape
        Bn = h_neigh.shape[0]
        msg = h_neigh[None, :, :] + E[edge_types]
        q = (h_target @ Wq.T + bq).reshape(Bt, H, DH)
        k = (msg @ Wk.T + bk).reshape(Bt, Bn, H, DH)
        v = (msg @ Wv.T + bv).reshape(Bt, Bn, H, DH)
        scores = jnp.einsum('bhd,bnhd->bhn', q, k) / np.sqrt(DH).astype(np.float32)
        mask = adjacency[:, None, :] == 0
        scores = jnp.where(mask, jnp.float32(-1000000000.0), scores)
        attn = jax.nn.softmax(scores, axis=-1)
        attn = jnp.where(mask, jnp.float32(0.0), attn)
        out = jnp.einsum('bhn,bnhd->bhd', attn, v).reshape(Bt, d)
        return out @ Wo.T + bo
    h = jnp.maximum(_layernorm(x, axis=-1), 0.0)
    x = x + _L0_gnn_ref(h, L0_gnn_h_neigh, adj, adj, L0_gnn_Wq, L0_gnn_bq, L0_gnn_Wk, L0_gnn_bk, L0_gnn_Wv, L0_gnn_bv, L0_gnn_Wo, L0_gnn_bo, L0_gnn_E)
    return x

_drawn_inputs = setup_inputs


def setup_inputs(seed=0):
    import zlib

    import numpy as np

    out = dict(_drawn_inputs(seed))
    spreads = {'L0_gnn_bq': (0.0, 0.368),
     'L0_gnn_bk': (0.0, 0.8),
     'L0_gnn_bv': (0.0, 0.1),
     'L0_gnn_bo': (0.0, 0.1)}
    factors = {}
    for name, (base, spread) in spreads.items():
        noise = np.random.default_rng([zlib.crc32(name.encode()), seed]).standard_normal(out[name].shape)
        drawn = base * np.exp(spread * noise) if base else spread * noise
        out[name] = jnp.asarray(drawn.astype(out[name].dtype))
    for name, factor in factors.items():
        out[name] = (out[name] * factor).astype(out[name].dtype)
    return out
```

```python
from contextlib import ExitStack

import concourse.bass as bass
from concourse import mybir

B, N, D, H = 512, 512, 128, 8
DH = D // H
P = 128
BT, NT = B // P, N // P
PARTS = 3
Q_SLOTS = (0, 1, 2, 0, 1, 0)
K_SLOTS = (0, 1, 0, 1, 0, 2)
PAIR_ROWS = DH * len(Q_SLOTS)
MAX_ROWS = 2
STACK = PAIR_ROWS + MAX_ROWS
G = 2
HG = H // G
CT = P // HG
MASKED = -(2.0**30)
FLOOR = -(2.0**29)
TINY = 1e-30
EPS = 1e-5
A_BANKS = (0, 1)
B_BANKS = (2, 3, 4)
ACC_BANK, MAX_BANK, MISC_BANK = 5, 6, 7
K_BANK, HT_BANK, Q_BANK, V_BANK = 0, 1, 2, 7


def gnn_kernel(nc, x_in, adj_b, adj_n, pack_k, pack_w, bias_rows, out):
    f32, bf16, i32 = mybir.dt.float32, mybir.dt.bfloat16, mybir.dt.int32
    ACT = mybir.ActivationFunctionType
    ALU = mybir.AluOpType

    ctx = ExitStack()
    with ctx:
        def sb(name, shape, dt=f32):
            return ctx.enter_context(nc.sbuf_tensor(name, shape, dt))

        def sem(name):
            return ctx.enter_context(nc.semaphore(name))

        part_dram = {
            "q": nc.dram_tensor("q_parts_dram", (PARTS, D, B), bf16, kind="Internal").ap(),
            "k": nc.dram_tensor("k_parts_dram", (PARTS, D, N), bf16, kind="Internal").ap(),
        }

        xt = sb("xt", [P, BT, D])
        xn = sb("xn", [P, BT, D])
        stats = sb("stats", [P, BT, 6])
        mean_var = sb("mean_var", [P, BT, 2])
        std = sb("std", [P, BT])
        rstd = sb("rstd", [P, BT])
        eps = sb("eps", [P, 1])
        warm = sb("warm", [P, 1])
        hT = sb("hT", [P, B])
        pk = sb("pk", [P, N + D + 4])
        hnT, wkT = pk[:, 0:N], pk[:, N:N + D]
        bq_col, bk_col, e1_col = (pk[:, N + D + i:N + D + i + 1] for i in range(3))
        pw = sb("pw", [P, 4 * D])
        wqT, wvT = pw[:, 0:D], pw[:, D:2 * D]
        brow = sb("brow", [P, 2 * D])
        bv_row, bo_row = brow[:, 0:D], brow[:, D:2 * D]
        msgT = sb("msgT", [P, N])
        full = {"q": sb("q_full", [P, B]), "k": sb("k_full", [P, N])}
        rest1 = {"q": sb("q_rest1", [P, B]), "k": sb("k_rest1", [P, N])}
        parts = {"q": sb("q_parts", [P, PARTS, B], bf16), "k": sb("k_parts", [P, PARTS, N], bf16)}
        QS = sb("QS", [P, H, B], bf16)
        KS = sb("KS", [P, H, N], bf16)
        adj_b_sb = sb("adj_b_sb", [P, BT * N], i32)
        adj_n_sb = sb("adj_n_sb", [P, NT * B], i32)
        mask_b = sb("mask_b", [P, BT, N], bf16)
        mask_n = sb("mask_n", [P, NT, B], bf16)
        V = sb("V", [P, NT, H, CT])
        masked_scores = sb("masked_scores", [P, len(A_BANKS), N], bf16)
        row_max = sb("row_max", [P, H, BT])
        neg_max = sb("neg_max", [P, H, BT, MAX_ROWS], bf16)
        prob = sb("prob", [P, H, NT, B])
        ident = sb("ident", [P, P])
        ident16 = sb("ident16", [P, P], bf16)
        pick_sum = sb("pick_sum", [P, HG])
        U = sb("U", [P, G, B])
        sums = sb("sums", [P, G, BT * HG])
        recip = sb("recip", [P, G, BT * HG])
        recip_rows = sb("recip_rows", [P, G, BT * P])
        ctxT = sb("ctxT", [P, G, B])
        resid = sb("resid", [P, BT, D])
        partial = sb("partial", [P, BT, D])
        y = sb("y", [P, BT, D])
        ps = ctx.enter_context(nc.psum_tensor("ps", [P, 8, 512], f32))

        x_loaded, pk_loaded, pw_loaded, rows_loaded = (
            sem("x_loaded"), sem("pk_loaded"), sem("pw_loaded"), sem("rows_loaded"))
        adj_b_loaded, adj_n_loaded = sem("adj_b_loaded"), sem("adj_n_loaded")
        part_written = {"q": sem("q_part_written"), "k": sem("k_part_written")}
        stacked = {"q": sem("q_stacked"), "k": sem("k_stacked")}
        stored = sem("stored")
        eps_set, idents_zero, idents_ready, pick_ready, ones_ready = (
            sem("eps_set"), sem("idents_zero"), sem("idents_ready"), sem("pick_ready"), sem("ones_ready"))
        msg_ready, stats_ready, mean_ready, std_ready, rstd_ready, xn_ready = (
            sem("msg_ready"), sem("stats_ready"), sem("mean_ready"), sem("std_ready"), sem("rstd_ready"),
            sem("xn_ready"))
        xT_ready, hT_ready = sem("xT_ready"), sem("hT_ready")
        projected = {"q": sem("q_projected"), "k": sem("k_projected")}
        full_ready = {"q": sem("q_full_ready"), "k": sem("k_full_ready")}
        part_ready = {"q": sem("q_part_ready"), "k": sem("k_part_ready")}
        rest_ready = {"q": sem("q_rest_ready"), "k": sem("k_rest_ready")}
        v_projected, v_ready = sem("v_projected"), sem("v_ready")
        mask_b_ready, mask_n_ready = sem("mask_b_ready"), sem("mask_n_ready")
        scores_b, max_found, high_ready, max_split, max_turned, max_placed = (
            sem("scores_b"), sem("max_found"), sem("high_ready"), sem("max_split"), sem("max_turned"),
            sem("max_placed"))
        scores_n, exp_done, pv_done, u_ready = sem("scores_n"), sem("exp_done"), sem("pv_done"), sem("u_ready")
        sums_turned, sums_safe, recip_ready, recip_repeated, recip_spread, ctx_ready = (
            sem("sums_turned"), sem("sums_safe"), sem("recip_ready"), sem("recip_repeated"), sem("recip_spread"),
            sem("ctx_ready"))
        out_projected, resid_ready, partial_ready, y_ready = (
            sem("out_projected"), sem("resid_ready"), sem("partial_ready"), sem("y_ready"))

        block = ctx.enter_context(nc.Block())

        @block.sync
        def _(sp):
            sp.dma_start(xt[:, :, :], x_in).then_inc(x_loaded, 16)
            sp.dma_start(pw[:, :], pack_w).then_inc(pw_loaded, 16)
            for name, stack, slots in (("k", KS, K_SLOTS), ("q", QS, Q_SLOTS)):
                for part in range(PARTS):
                    sp.wait_ge(part_ready[name], part + 1)
                    sp.dma_start(part_dram[name][part], parts[name][:, part, :]).then_inc(part_written[name], 16)
                for part in range(PARTS):
                    if part == 0:
                        sp.wait_ge(part_written[name], 16 * PARTS)
                    for slot in range(len(slots)):
                        if slots[slot] == part:
                            sp.dma_start(
                                stack[DH * slot:DH * (slot + 1), :, :],
                                part_dram[name][part].rearrange("(d h) b -> d h b", h=H),
                            ).then_inc(stacked[name], 16)
            sp.wait_ge(y_ready, 1)
            sp.dma_start(out, y[:, :, :]).then_inc(stored, 16)
            sp.wait_ge(stored, 16)

        @block.gpsimd
        def _(pool):
            nc.gpsimd.memset(eps[:, :], EPS).then_inc(eps_set, 1)
            nc.gpsimd.memset(ident[:, :], 0.0)
            nc.gpsimd.memset(ident16[:, :], 0.0)
            nc.gpsimd.memset(pick_sum[:, :], 0.0).then_inc(idents_zero, 1)
            pool.wait_ge(idents_zero, 1)
            for m in (ident, ident16):
                last = nc.gpsimd.affine_select(out=m[:, :], in_=m[:, :], compare_op=ALU.not_equal, fill=1.0, base=0,
                                               pattern=[[-1, P]], channel_multiplier=1)
            last.then_inc(idents_ready, 1)
            nc.gpsimd.affine_select(out=pick_sum[:, :], in_=pick_sum[:, :], compare_op=ALU.not_equal, fill=1.0,
                                    base=-DH, pattern=[[-CT, HG]], channel_multiplier=1).then_inc(pick_ready, 1)
            nc.gpsimd.memset(V[:, :, :, :], 1.0).then_inc(ones_ready, 1)
            pool.wait_ge(ones_ready, 1)
            nc.gpsimd.memset(KS[PAIR_ROWS:STACK, :, :], 1.0).then_inc(ones_ready, 1)
            pool.wait_ge(ones_ready, 2)
            pool.wait_ge(x_loaded, 16)
            pool.wait_ge(rows_loaded, 16)
            nc.gpsimd.tensor_tensor(resid[:, :, :], xt[:, :, :],
                                    bo_row.rearrange("p (t c) -> p t c", t=1).to_broadcast([P, BT, D]),
                                    ALU.add).then_inc(resid_ready, 1)

        @block.scalar
        def _(act):
            act.dma_start(pk[:, :], pack_k).then_inc(pk_loaded, 16)
            act.dma_start(adj_b_sb[:, :], adj_b).then_inc(adj_b_loaded, 16)
            act.dma_start(adj_n_sb[:, :], adj_n).then_inc(adj_n_loaded, 16)
            act.dma_start(brow[:, :], bias_rows.to_broadcast([P, 2 * D])).then_inc(rows_loaded, 16)
            act.wait_ge(projected["k"], 1)
            nc.scalar.activation(full["k"][:, :], ps[:, K_BANK, :], ACT.Identity, bias=bk_col).then_inc(
                full_ready["k"], 1)
            act.wait_ge(eps_set, 1)
            act.wait_ge(mean_ready, 1)
            nc.scalar.activation(std[:, :], mean_var[:, :, 1], ACT.Sqrt, bias=eps[:, :]).then_inc(std_ready, 1)
            nc.scalar.activation(warm[:, :], eps[:, :], ACT.Exp)
            act.wait_ge(xT_ready, 1)
            nc.scalar.activation(hT[:, :], ps[:, HT_BANK, :], ACT.Relu).then_inc(hT_ready, 1)
            act.wait_ge(projected["q"], 1)
            nc.scalar.activation(full["q"][:, :], ps[:, Q_BANK, :], ACT.Identity, bias=bq_col).then_inc(
                full_ready["q"], 1)

            def place_max(h):
                act.wait_ge(max_turned, h + 1)
                nc.scalar.activation(QS[PAIR_ROWS:STACK, h, :], ps[PAIR_ROWS:STACK, MAX_BANK, :],
                                     ACT.Copy).then_inc(max_placed, 1)

            def take_pv(g):
                act.wait_ge(pv_done, g + 1)
                nc.scalar.activation(U[:, g, :], ps[:, ACC_BANK, :], ACT.Copy).then_inc(u_ready, 1)

            place_max(0)
            for h in range(H):
                for t in range(NT):
                    k = h * NT + t
                    act.wait_ge(scores_n, k + 1)
                    nc.scalar.activation(prob[:, h, t, :], ps[:, B_BANKS[k % len(B_BANKS)], :], ACT.Exp,
                                         scale=DH ** -0.5).then_inc(exp_done, 1)
                    if t == 1 and h + 1 < H:
                        place_max(h + 1)
                    if t == 0 and h == HG + 2:
                        take_pv(0)
            take_pv(1)

        @block.vector
        def _(dve):
            def split(name):
                dve.wait_ge(full_ready[name], 1)
                nc.vector.tensor_copy(parts[name][:, 0, :], full[name][:, :]).then_inc(part_ready[name], 1)
                dve.wait_ge(part_ready[name], 1)
                nc.vector.tensor_tensor(rest1[name][:, :], full[name][:, :], parts[name][:, 0, :],
                                        ALU.subtract).then_inc(rest_ready[name], 1)
                dve.wait_ge(rest_ready[name], 1)
                nc.vector.tensor_copy(parts[name][:, 1, :], rest1[name][:, :]).then_inc(part_ready[name], 1)
                dve.wait_ge(part_ready[name], 2)
                nc.vector.tensor_tensor(parts[name][:, 2, :], rest1[name][:, :], parts[name][:, 1, :],
                                        ALU.subtract).then_inc(part_ready[name], 1)

            dve.wait_ge(pk_loaded, 16)
            nc.vector.tensor_scalar(msgT[:, :], hnT, e1_col, None, ALU.add).then_inc(msg_ready, 1)
            dve.wait_ge(x_loaded, 16)
            for t in range(BT):
                last = nc.vector.bn_stats(stats[:, t, :], xt[:, t, :])
            last.then_inc(stats_ready, 1)
            dve.wait_ge(stats_ready, 1)
            for t in range(BT):
                last = nc.vector.bn_aggr(mean_var[:, t, :], stats[:, t, :])
            last.then_inc(mean_ready, 1)
            dve.wait_ge(std_ready, 1)
            nc.vector.reciprocal(rstd[:, :], std[:, :]).then_inc(rstd_ready, 1)
            dve.wait_ge(rstd_ready, 1)
            for t in range(BT):
                nc.vector.tensor_scalar(xn[:, t, :], xt[:, t, :], mean_var[:, t, 0:1], rstd[:, t:t + 1],
                                        ALU.subtract, ALU.mult).then_inc(xn_ready, 1)
            split("k")
            split("q")
            dve.wait_ge(adj_b_loaded, 16)
            nc.vector.tensor_scalar(mask_b[:, :, :], adj_b_sb[:, :].rearrange("p (t n) -> p t n", t=BT), 0.0, MASKED,
                                    ALU.is_equal, ALU.mult).then_inc(mask_b_ready, 1)
            dve.wait_ge(adj_n_loaded, 16)
            nc.vector.tensor_scalar(mask_n[:, :, :], adj_n_sb[:, :].rearrange("p (t b) -> p t b", t=NT), 0.0, MASKED,
                                    ALU.is_equal, ALU.mult).then_inc(mask_n_ready, 1)
            dve.wait_ge(v_projected, 1)
            dve.wait_ge(ones_ready, 1)
            dve.wait_ge(rows_loaded, 16)
            for t in range(NT):
                last = nc.vector.tensor_tensor(
                    V[:, t, :, 0:DH], ps[:, V_BANK, t * D:(t + 1) * D].rearrange("p (h d) -> p h d", h=H),
                    bv_row.rearrange("p (h d) -> p h d", h=H), ALU.add)
            last.then_inc(v_ready, 1)

            dve.wait_ge(mask_b_ready, 1)
            for h in range(H):
                for t in range(BT):
                    k = h * BT + t
                    dve.wait_ge(scores_b, k + 1)
                    nc.vector.tensor_tensor_reduce(
                        out=masked_scores[:, k % len(A_BANKS), :], in0=ps[:, A_BANKS[k % len(A_BANKS)], :], in1=mask_b[:, t, :],
                        scale=1.0, scalar=FLOOR, op0=ALU.add, op1=ALU.max,
                        accum_out=row_max[:, h, t:t + 1]).then_inc(max_found, 1)
                dve.wait_ge(max_found, (h + 1) * BT)
                nc.vector.tensor_scalar(neg_max[:, h, :, 0], row_max[:, h, :], -1.0, None,
                                        ALU.mult).then_inc(high_ready, 1)
                dve.wait_ge(high_ready, h + 1)
                nc.vector.scalar_tensor_tensor(out=neg_max[:, h, :, 1], in0=row_max[:, h, :], scalar=-1.0,
                                               in1=neg_max[:, h, :, 0], op0=ALU.mult,
                                               op1=ALU.subtract).then_inc(max_split, 1)

            for g in range(G):
                dve.wait_ge(sums_turned, g + 1)
                nc.vector.tensor_scalar(sums[:, g, :], ps[:, MISC_BANK, 0:BT * HG], TINY, None,
                                        ALU.max).then_inc(sums_safe, 1)
                dve.wait_ge(sums_safe, g + 1)
                nc.vector.reciprocal(recip[:, g, :], sums[:, g, :]).then_inc(recip_ready, 1)
                dve.wait_ge(recip_ready, g + 1)
                nc.vector.tensor_copy(
                    recip_rows[:, g, :].rearrange("p (j c) -> p j c", c=CT),
                    recip[:, g, :].rearrange("p (j c) -> p j c", c=1).to_broadcast([P, BT * HG, CT]),
                ).then_inc(recip_repeated, 1)
                dve.wait_ge(recip_spread, g + 1)
                nc.vector.tensor_tensor(ctxT[:, g, :], ps[:, MISC_BANK, :], U[:, g, :],
                                        ALU.mult).then_inc(ctx_ready, 1)
                dve.wait_ge(out_projected, g + 1)
                product = ps[:, MISC_BANK, :].rearrange("p (t c) -> p t c", t=BT)
                if g == 0:
                    dve.wait_ge(resid_ready, 1)
                    nc.vector.tensor_tensor(partial[:, :, :], product, resid[:, :, :], ALU.add).then_inc(
                        partial_ready, 1)
                else:
                    dve.wait_ge(partial_ready, 1)
                    nc.vector.tensor_tensor(y[:, :, :], product, partial[:, :, :], ALU.add).then_inc(y_ready, 1)

        @block.tensor
        def _(pe):
            pe.wait_ge(pk_loaded, 16)
            pe.wait_ge(msg_ready, 1)
            nc.tensor.matmul(ps[:, K_BANK, :], wkT, msgT[:, :], start=True, stop=True).then_inc(projected["k"], 1)
            pe.wait_ge(pw_loaded, 16)
            for t in range(NT):
                last = nc.tensor.matmul(ps[:, V_BANK, t * D:(t + 1) * D], msgT[:, t * P:(t + 1) * P], wvT,
                                        start=True, stop=True)
            last.then_inc(v_projected, 1)
            pe.wait_ge(idents_ready, 1)
            for t in range(BT):
                pe.wait_ge(xn_ready, t + 1)
                last = nc.tensor.transpose(ps[:, HT_BANK, t * P:(t + 1) * P], xn[:, t, :], ident[:, :])
            last.then_inc(xT_ready, 1)
            pe.wait_ge(hT_ready, 1)
            nc.tensor.matmul(ps[:, Q_BANK, :], wqT, hT[:, :], start=True, stop=True).then_inc(projected["q"], 1)

            def score_by_target(h, t):
                k = h * BT + t
                if k >= len(A_BANKS):
                    pe.wait_ge(max_found, k + 1 - len(A_BANKS))
                nc.tensor.matmul(ps[:, A_BANKS[k % len(A_BANKS)], :], QS[0:PAIR_ROWS, h, t * P:(t + 1) * P],
                                 KS[0:PAIR_ROWS, h, :], start=True, stop=True).then_inc(scores_b, 1)

            def turn_max(h):
                pe.wait_ge(max_split, h + 1)
                if h >= 1:
                    pe.wait_ge(max_placed, h)
                for t in range(BT):
                    last = nc.tensor.matmul(ps[PAIR_ROWS:STACK, MAX_BANK, t * P:(t + 1) * P], neg_max[:, h, t, :],
                                            ident16[:, :], start=True, stop=True)
                last.then_inc(max_turned, 1)

            def score_by_neighbour(h, t):
                k = h * NT + t
                bank = ps[:, B_BANKS[k % len(B_BANKS)], :]
                if k >= len(B_BANKS):
                    pe.wait_ge(exp_done, k + 1 - len(B_BANKS))
                nc.tensor.matmul(bank, ident16[:, :], mask_n[:, t, :], start=True, stop=False)
                if t == 0:
                    pe.wait_ge(max_placed, h + 1)
                nc.tensor.matmul(bank, KS[0:STACK, h, t * P:(t + 1) * P], QS[0:STACK, h, :], start=False,
                                 stop=True).then_inc(scores_n, 1)

            def product_with_v(g, t):
                if g == 1 and t == 0:
                    pe.wait_ge(u_ready, 1)
                pe.wait_ge(exp_done, ((g + 1) * HG - 1) * NT + t + 1)
                for j in range(HG):
                    h = g * HG + j
                    last = nc.tensor.matmul(ps[j * CT:(j + 1) * CT, ACC_BANK, :], V[:, t, h, :], prob[:, h, t, :],
                                            start=t == 0, stop=t == NT - 1, tile_position=(0, j * CT))
                if t == NT - 1:
                    last.then_inc(pv_done, 1)

            def turn_sums(g):
                pe.wait_ge(u_ready, g + 1)
                if g == 1:
                    pe.wait_ge(partial_ready, 1)
                for t in range(BT):
                    last = nc.tensor.matmul(ps[:, MISC_BANK, t * HG:(t + 1) * HG], U[:, g, t * P:(t + 1) * P],
                                            pick_sum[:, :], start=True, stop=True)
                last.then_inc(sums_turned, 1)

            def spread_recip(g):
                pe.wait_ge(recip_repeated, g + 1)
                for t in range(BT):
                    last = nc.tensor.matmul(ps[:, MISC_BANK, t * P:(t + 1) * P],
                                            recip_rows[:, g, t * P:(t + 1) * P], ident[:, :], start=True, stop=True)
                last.then_inc(recip_spread, 1)

            def project_out(g):
                pe.wait_ge(ctx_ready, g + 1)
                for t in range(BT):
                    last = nc.tensor.matmul(ps[:, MISC_BANK, t * D:(t + 1) * D], ctxT[:, g, t * P:(t + 1) * P],
                                            pw[:, (2 + g) * D:(3 + g) * D], start=True, stop=True)
                last.then_inc(out_projected, 1)

            pe.wait_ge(stacked["k"], 16 * len(K_SLOTS))
            pe.wait_ge(stacked["q"], 16 * len(Q_SLOTS))
            for h in range(2):
                for t in range(BT):
                    score_by_target(h, t)
                if h == 0:
                    turn_max(0)
            pe.wait_ge(mask_n_ready, 1)
            pe.wait_ge(ones_ready, 2)
            pe.wait_ge(v_ready, 1)
            pe.wait_ge(pick_ready, 1)
            for h in range(H):
                for t in range(NT):
                    if h + 2 < H:
                        score_by_target(h + 2, t)
                    if t == 1 and h + 1 < H:
                        turn_max(h + 1)
                    score_by_neighbour(h, t)
                    if h in (HG, HG + 1) and t % 2:
                        product_with_v(0, 2 * (h - HG) + t // 2)
                    if h == HG + 2 and t == 3:
                        turn_sums(0)
                    if h == HG + 3 and t == 1:
                        spread_recip(0)
                    if h == HG + 3 and t == 3:
                        project_out(0)
            for t in range(NT):
                product_with_v(1, t)
            turn_sums(1)
            spread_recip(1)
            project_out(1)


def kernel(x, adj, L0_gnn_h_neigh, L0_gnn_Wq, L0_gnn_bq, L0_gnn_Wk, L0_gnn_bk, L0_gnn_Wv, L0_gnn_bv, L0_gnn_Wo,
           L0_gnn_bo, L0_gnn_E):
    import numpy as np
    import concourse.bacc as bacc
    from concourse.bass_utils import run_bass_kernel_spmd

    x, adj, hn = np.asarray(x), np.asarray(adj), np.asarray(L0_gnn_h_neigh)
    Wq, Wk, Wv, Wo = (np.asarray(w) for w in (L0_gnn_Wq, L0_gnn_Wk, L0_gnn_Wv, L0_gnn_Wo))
    bq, bk, bv, bo = (np.asarray(b) for b in (L0_gnn_bq, L0_gnn_bk, L0_gnn_bv, L0_gnn_bo))
    E = np.asarray(L0_gnn_E)

    def by_dim(w):
        return w.reshape(H, DH, -1).transpose(1, 0, 2).reshape(D, -1)

    wo = np.zeros((G, HG, CT, D), Wo.dtype)
    wo[:, :, :DH] = Wo.T.reshape(G, HG, DH, D)
    cols = [by_dim(bq), by_dim(bk), E[1][:, None], np.zeros((D, 1), E.dtype)]
    arrays = {
        "x_dram": x.reshape(P, BT * D),
        "adj_b_dram": adj.reshape(P, BT * N),
        "adj_n_dram": adj.reshape(P, BT, NT, P).transpose(3, 2, 1, 0).reshape(P, NT * B),
        "pack_k_dram": np.concatenate([hn.T, by_dim(Wk).T, *cols], axis=1),
        "pack_w_dram": np.concatenate([by_dim(Wq).T, Wv.T, *wo.reshape(G, P, D)], axis=1),
        "bias_rows_dram": np.concatenate([bv, bo])[None],
    }
    arrays = {n: np.ascontiguousarray(a) for n, a in arrays.items()}
    nc = bacc.Bacc("TRN2", target_bir_lowering=False, num_devices=1)
    args = [nc.dram_tensor(n, a.shape, mybir.dt.from_np(a.dtype), kind="ExternalInput").ap() for n, a in arrays.items()]
    out = nc.dram_tensor("out_dram", (P, BT * D), mybir.dt.float32, kind="ExternalOutput").ap()
    gnn_kernel(nc, *args, out)
    r = run_bass_kernel_spmd(nc, [arrays], core_ids=[0])
    return r.results[0]["out_dram"].reshape(B, D)
```

```python
from contextlib import ExitStack

import concourse.bass as bass
from concourse import mybir

B, N, D, H = 512, 512, 128, 8
DH = D // H
P = 128
BT, NT = B // P, N // P
PARTS = 3
Q_SLOTS = (0, 1, 2, 0, 1, 0)
K_SLOTS = (2, 1, 0, 1, 0, 0)
Q_PLACES = (0, 1, 2)
K_PLACES = (2, 1, 0)
SLOT_RUNS = ((0, 3), (3, 2), (5, 1))
PICKED = 2
PAIR_ROWS = DH * len(Q_SLOTS)
MAX_ROWS = 2
STACK = PAIR_ROWS + MAX_ROWS
G = 2
HG = H // G
CT = P // HG
MASKED = -(2.0**30)
FLOOR = -(2.0**29)
TINY = 1e-30
EPS = 1e-5
A_BANKS = (0, 1)
A_AHEAD = 6
B_BANKS = (2, 3, 4)
ACC_BANK, MAX_BANK, MISC_BANK = 5, 6, 7
PV_AT = HG * NT + 1
K_BANK, Q_BANK, HT_BANK, WARM_BANK, V_BANK = 0, 2, 3, 6, 7
PICK_BANKS = {"k": (4, 5), "q": (6, 4)}
HALVES = 2
HB, HT_TILES = B // HALVES, BT // HALVES
TAIL_ACC, TAIL_SUMS, TAIL_SPREAD, TAIL_OUT = (5, 0), (1, 6), (7, 2), (3, 4)
WARM_UP = 10


def gnn_kernel(nc, x_in, adj_b, adj_n, pack_k, pack_w, bias_rows, out):
    f32, bf16, i32 = mybir.dt.float32, mybir.dt.bfloat16, mybir.dt.int32
    ACT = mybir.ActivationFunctionType
    ALU = mybir.AluOpType

    ctx = ExitStack()
    with ctx:
        def sb(name, shape, dt=f32):
            return ctx.enter_context(nc.sbuf_tensor(name, shape, dt))

        def sem(name):
            return ctx.enter_context(nc.semaphore(name))

        part_dram = {
            "q": nc.dram_tensor("q_parts_dram", (PARTS, D, B), bf16, kind="Internal").ap(),
            "k": nc.dram_tensor("k_parts_dram", (PARTS, D, N), bf16, kind="Internal").ap(),
        }

        xt = sb("xt", [P, BT, D])
        xn = sb("xn", [P, BT, D])
        stats = sb("stats", [P, BT, 6])
        mean_var = sb("mean_var", [P, BT, 2])
        std = sb("std", [P, BT])
        rstd = sb("rstd", [P, BT])
        eps = sb("eps", [P, 1])
        warm = sb("warm", [P, 1])
        warm2 = sb("warm2", [P, 1])
        hT = sb("hT", [P, B])
        pk = sb("pk", [P, N + D + 4])
        hnT, wkT = pk[:, 0:N], pk[:, N:N + D]
        bq_col, bk_col, e1_col = (pk[:, N + D + i:N + D + i + 1] for i in range(3))
        pw = sb("pw", [P, 4 * D])
        wqT, wvT = pw[:, 0:D], pw[:, D:2 * D]
        brow = sb("brow", [P, 2 * D])
        bv_row, bo_row = brow[:, 0:D], brow[:, D:2 * D]
        msgT = sb("msgT", [P, N])
        parts = {"q": sb("q_parts", [P, PARTS, B], bf16), "k": sb("k_parts", [P, PARTS, N], bf16)}
        QS = sb("QS", [P, H, B], bf16)
        KS = sb("KS", [P, H, N], bf16)
        adj_b_sb = sb("adj_b_sb", [P, BT * N], i32)
        adj_n_sb = sb("adj_n_sb", [P, NT * B], i32)
        mask_b = sb("mask_b", [P, BT, N], bf16)
        mask_n = sb("mask_n", [P, NT, B], bf16)
        V = sb("V", [P, NT, H, CT])
        masked_scores = sb("masked_scores", [P, len(A_BANKS), N], bf16)
        row_max = sb("row_max", [P, H, BT])
        neg_max = sb("neg_max", [P, H, BT, MAX_ROWS], bf16)
        prob = sb("prob", [P, H, NT, B])
        ident = sb("ident", [P, P])
        ident16 = sb("ident16", [P, P], bf16)
        minus16 = sb("minus16", [P, P], bf16)
        warm_up = sb("warm_up", [P, 512], bf16)
        pick = {"q": sb("q_pick", [P, PARTS, PICKED, PAIR_ROWS], bf16),
                "k": sb("k_pick", [P, PARTS, PICKED, PAIR_ROWS], bf16)}
        pick_sum = sb("pick_sum", [P, HG])
        U = sb("U", [P, G, B])
        sums = sb("sums", [P, G, BT * HG])
        recip = sb("recip", [P, G, BT * HG])
        recip_rows = sb("recip_rows", [P, G, BT * P])
        ctxT = sb("ctxT", [P, G, B])
        resid = sb("resid", [P, BT, D])
        partial = sb("partial", [P, BT, D])
        y = sb("y", [P, BT, D])
        ps = ctx.enter_context(nc.psum_tensor("ps", [P, 8, 512], f32))

        x_loaded, pk_loaded, pw_loaded, rows_loaded = (
            sem("x_loaded"), sem("pk_loaded"), sem("pw_loaded"), sem("rows_loaded"))
        adj_b_loaded, adj_n_loaded = sem("adj_b_loaded"), sem("adj_n_loaded")
        part_written = {"q": sem("q_part_written"), "k": sem("k_part_written")}
        stacked = {"q": sem("q_stacked"), "k": sem("k_stacked")}
        stored = [sem(f"stored{i}") for i in range(HALVES)]
        eps_set, idents_zero, idents_ready, pick_ready, ones_ready = (
            sem("eps_set"), sem("idents_zero"), sem("idents_ready"), sem("pick_ready"), sem("ones_ready"))
        msg_ready, stats_ready, mean_ready, std_ready, rstd_ready, xn_ready = (
            sem("msg_ready"), sem("stats_ready"), sem("mean_ready"), sem("std_ready"), sem("rstd_ready"),
            sem("xn_ready"))
        xT_ready, hT_ready = sem("xT_ready"), sem("hT_ready")
        projected = {"q": sem("q_projected"), "k": sem("k_projected")}
        part_ready = {"q": sem("q_part_ready"), "k": sem("k_part_ready")}
        part_taken = {"q": sem("q_part_taken"), "k": sem("k_part_taken")}
        picked = {"q": sem("q_picked"), "k": sem("k_picked")}
        pick_placed = {"q": sem("q_pick_placed"), "k": sem("k_pick_placed")}
        warm_set, picks_zero, picks_set = sem("warm_set"), sem("picks_zero"), sem("picks_set")
        v_projected, v_ready = sem("v_projected"), sem("v_ready")
        mask_b_ready, mask_n_ready = sem("mask_b_ready"), sem("mask_n_ready")
        scores_b, max_found, high_ready, max_split, max_turned, max_placed = (
            sem("scores_b"), sem("max_found"), sem("high_ready"), sem("max_split"), sem("max_turned"),
            sem("max_placed"))
        scores_n, exp_done, pv_done, u_ready = sem("scores_n"), sem("exp_done"), sem("pv_done"), sem("u_ready")
        sums_turned, sums_safe, recip_ready, recip_repeated, recip_spread, ctx_ready = (
            sem("sums_turned"), sem("sums_safe"), sem("recip_ready"), sem("recip_repeated"), sem("recip_spread"),
            sem("ctx_ready"))
        out_projected, resid_ready, partial_ready, y_ready = (
            sem("out_projected"), sem("resid_ready"), sem("partial_ready"), sem("y_ready"))

        block = ctx.enter_context(nc.Block())

        @block.sync
        def _(sp):
            sp.dma_start(xt[:, :, :], x_in).then_inc(x_loaded, 16)
            sp.dma_start(pw[:, :], pack_w).then_inc(pw_loaded, 16)
            for name, stack, slots, places in (("k", KS, K_SLOTS, K_PLACES), ("q", QS, Q_SLOTS, Q_PLACES)):
                sp.wait_ge(part_ready[name], PARTS)
                sp.dma_start(part_dram[name].rearrange("s f b -> f s b"), parts[name][:, :, :]).then_inc(
                    part_written[name], 16)
                sp.wait_ge(part_written[name], 16)
                rows = part_dram[name].rearrange("s (d h) b -> (s d) h b", h=H)
                for slot, length in SLOT_RUNS:
                    place = places[slots[slot]]
                    sp.dma_start(stack[DH * slot:DH * (slot + length), PICKED:H, :],
                                 rows[DH * place:DH * (place + length), PICKED:H, :]).then_inc(stacked[name], 16)
            sp.wait_ge(y_ready, 1)
            sp.dma_start(out[:, 0:HT_TILES * D], y[:, 0:HT_TILES, :]).then_inc(stored[0], 16)
            sp.wait_ge(stored[0], 16)

        @block.gpsimd
        def _(pool):
            nc.gpsimd.memset(eps[:, :], EPS).then_inc(eps_set, 1)
            nc.gpsimd.memset(ident[:, :], 0.0)
            nc.gpsimd.memset(ident16[:, :], 0.0)
            nc.gpsimd.memset(minus16[:, :], 0.0)
            nc.gpsimd.memset(pick_sum[:, :], 0.0).then_inc(idents_zero, 1)
            pool.wait_ge(idents_zero, 1)
            for m, value in ((ident16, 1.0), (ident, 1.0), (minus16, -1.0)):
                nc.gpsimd.affine_select(out=m[:, :], in_=m[:, :], compare_op=ALU.not_equal, fill=value, base=0,
                                        pattern=[[-1, P]], channel_multiplier=1).then_inc(idents_ready, 1)
            nc.gpsimd.affine_select(out=pick_sum[:, :], in_=pick_sum[:, :], compare_op=ALU.not_equal, fill=1.0,
                                    base=-DH, pattern=[[-CT, HG]], channel_multiplier=1).then_inc(pick_ready, 1)
            nc.gpsimd.memset(V[:, :, :, :], 1.0).then_inc(ones_ready, 1)
            pool.wait_ge(ones_ready, 1)
            nc.gpsimd.memset(KS[PAIR_ROWS:STACK, :, :], 1.0).then_inc(ones_ready, 1)
            pool.wait_ge(ones_ready, 2)
            pool.wait_ge(x_loaded, 16)
            pool.wait_ge(rows_loaded, 16)
            nc.gpsimd.tensor_tensor(resid[:, :, :], xt[:, :, :],
                                    bo_row.rearrange("p (t c) -> p t c", t=1).to_broadcast([P, BT, D]),
                                    ALU.add).then_inc(resid_ready, 1)

        @block.scalar
        def _(act):
            act.dma_start(pk[:, :], pack_k).then_inc(pk_loaded, 16)
            act.dma_start(brow[:, :], bias_rows.to_broadcast([P, 2 * D])).then_inc(rows_loaded, 16)
            act.dma_start(adj_b_sb[:, :], adj_b).then_inc(adj_b_loaded, 16)
            act.dma_start(adj_n_sb[:, :], adj_n).then_inc(adj_n_loaded, 16)
            act.wait_ge(eps_set, 1)
            nc.scalar.activation(warm[:, :], eps[:, :], ACT.Sqrt)

            def take_part(name, bank, bias, place, n):
                if n == 0:
                    act.wait_ge(projected[name], 1)
                else:
                    act.wait_ge(part_taken[name], n)
                nc.scalar.activation(parts[name][:, place, :], ps[:, bank, :], ACT.Identity, bias=bias).then_inc(
                    part_ready[name], 1)

            act.wait_ge(mean_ready, 1)
            nc.scalar.activation(std[:, :], mean_var[:, :, 1], ACT.Sqrt, bias=eps[:, :]).then_inc(std_ready, 1)
            for n in range(PARTS):
                take_part("k", K_BANK, bk_col, K_PLACES[n], n)
            for n in range(PARTS):
                take_part("q", Q_BANK, bq_col, Q_PLACES[n], n)
            act.wait_ge(picked["q"], 1)
            nc.scalar.activation(QS[0:PAIR_ROWS, 0, :], ps[0:PAIR_ROWS, PICK_BANKS["q"][0], :], ACT.Copy).then_inc(
                pick_placed["q"], 1)
            nc.scalar.activation(warm2[:, :], eps[:, :], ACT.Exp)

            def place_max(h):
                act.wait_ge(max_turned, h + 1)
                nc.scalar.activation(QS[PAIR_ROWS:STACK, h, :], ps[PAIR_ROWS:STACK, MAX_BANK, :],
                                     ACT.Copy).then_inc(max_placed, 1)

            place_max(0)
            for h in range(H):
                for t in range(NT):
                    k = h * NT + t
                    act.wait_ge(scores_n, k + 1)
                    nc.scalar.activation(prob[:, h, t, :], ps[:, B_BANKS[k % len(B_BANKS)], :], ACT.Exp,
                                         scale=DH ** -0.5).then_inc(exp_done, 1)
                    if t == 2 and h + 1 < H:
                        place_max(h + 1)
                    if k == PV_AT + 2 * NT - 1:
                        act.wait_ge(pv_done, 1)
                        nc.scalar.activation(U[:, 0, :], ps[:, ACC_BANK, :], ACT.Copy).then_inc(u_ready, 1)
            for i in range(HALVES):
                act.wait_ge(pv_done, 2 + i)
                nc.scalar.activation(U[:, 1, i * HB:(i + 1) * HB], ps[:, TAIL_ACC[i], 0:HB], ACT.Copy).then_inc(
                    u_ready, 1)
            act.wait_ge(y_ready, 2)
            act.dma_start(out[:, HT_TILES * D:BT * D], y[:, HT_TILES:BT, :]).then_inc(stored[1], 16)
            act.wait_ge(stored[1], 16)

        @block.vector
        def _(dve):
            nc.vector.memset(warm_up[:, :], 1.0).then_inc(warm_set, 1)
            nc.vector.memset(pick["q"][:, :, :, :], 0.0).then_inc(picks_zero, 1)
            nc.vector.memset(pick["k"][:, :, :, :], 0.0).then_inc(picks_zero, 1)
            dve.wait_ge(picks_zero, 2)
            dve.wait_ge(idents_ready, 1)
            by_head = ident16[:, :].rearrange("p (d h) -> p h d", h=H)
            for name, slots in (("q", Q_SLOTS), ("k", K_SLOTS)):
                for slot in range(len(slots)):
                    last = nc.vector.tensor_copy(
                        pick[name][:, slots[slot], :, DH * slot:DH * (slot + 1)], by_head[:, 0:PICKED, :])
            last.then_inc(picks_set, 1)
            dve.wait_ge(x_loaded, 16)
            for t in range(BT):
                last = nc.vector.bn_stats(stats[:, t, :], xt[:, t, :])
            last.then_inc(stats_ready, 1)
            dve.wait_ge(stats_ready, 1)
            for t in range(BT):
                last = nc.vector.bn_aggr(mean_var[:, t, :], stats[:, t, :])
            last.then_inc(mean_ready, 1)
            dve.wait_ge(pk_loaded, 16)
            nc.vector.tensor_scalar(msgT[:, :], hnT, e1_col, None, ALU.add).then_inc(msg_ready, 1)
            dve.wait_ge(std_ready, 1)
            nc.vector.reciprocal(rstd[:, :], std[:, :]).then_inc(rstd_ready, 1)
            dve.wait_ge(mean_ready, 1)
            dve.wait_ge(rstd_ready, 1)
            for t in range(BT):
                nc.vector.tensor_scalar(xn[:, t, :], xt[:, t, :], mean_var[:, t, 0:1], rstd[:, t:t + 1],
                                        ALU.subtract, ALU.mult).then_inc(xn_ready, 1)
            dve.wait_ge(xT_ready, 1)
            nc.vector.tensor_scalar(hT[:, :], ps[:, HT_BANK, :], 0.0, None, ALU.max).then_inc(hT_ready, 1)
            dve.wait_ge(adj_b_loaded, 16)
            nc.vector.tensor_scalar(mask_b[:, :, :], adj_b_sb[:, :].rearrange("p (t n) -> p t n", t=BT), 0.0, MASKED,
                                    ALU.is_equal, ALU.mult).then_inc(mask_b_ready, 1)
            for h in range(PICKED):
                dve.wait_ge(picked["k"], h + 1)
                nc.vector.tensor_copy(KS[0:PAIR_ROWS, h, :], ps[0:PAIR_ROWS, PICK_BANKS["k"][h], :]).then_inc(
                    pick_placed["k"], 1)
            dve.wait_ge(picked["q"], 2)
            nc.vector.tensor_copy(QS[0:PAIR_ROWS, 1, :], ps[0:PAIR_ROWS, PICK_BANKS["q"][1], :]).then_inc(
                pick_placed["q"], 1)

            def late_setup():
                dve.wait_ge(adj_n_loaded, 16)
                nc.vector.tensor_scalar(mask_n[:, :, :], adj_n_sb[:, :].rearrange("p (t b) -> p t b", t=NT), 0.0,
                                        MASKED, ALU.is_equal, ALU.mult).then_inc(mask_n_ready, 1)
                dve.wait_ge(v_projected, 1)
                dve.wait_ge(ones_ready, 1)
                dve.wait_ge(rows_loaded, 16)
                for t in range(NT):
                    last = nc.vector.tensor_tensor(
                        V[:, t, :, 0:DH], ps[:, V_BANK, t * D:(t + 1) * D].rearrange("p (h d) -> p h d", h=H),
                        bv_row.rearrange("p (h d) -> p h d", h=H), ALU.add)
                last.then_inc(v_ready, 1)

            late_setup()
            dve.wait_ge(mask_b_ready, 1)
            for h in range(H):
                for t in range(BT):
                    k = h * BT + t
                    dve.wait_ge(scores_b, k + 1)
                    nc.vector.tensor_tensor_reduce(
                        out=masked_scores[:, k % len(A_BANKS), :], in0=ps[:, A_BANKS[k % len(A_BANKS)], :], in1=mask_b[:, t, :],
                        scale=1.0, scalar=FLOOR, op0=ALU.add, op1=ALU.max,
                        accum_out=row_max[:, h, t:t + 1]).then_inc(max_found, 1)
                dve.wait_ge(max_found, (h + 1) * BT)
                nc.vector.tensor_scalar(neg_max[:, h, :, 0], row_max[:, h, :], -1.0, None,
                                        ALU.mult).then_inc(high_ready, 1)
                dve.wait_ge(high_ready, h + 1)
                nc.vector.scalar_tensor_tensor(out=neg_max[:, h, :, 1], in0=row_max[:, h, :], scalar=-1.0,
                                               in1=neg_max[:, h, :, 0], op0=ALU.mult,
                                               op1=ALU.subtract).then_inc(max_split, 1)

            def invert_sums(step, bank, g, first, tiles):
                at = slice(first * HG, (first + tiles) * HG)
                dve.wait_ge(sums_turned, step + 1)
                nc.vector.tensor_scalar(sums[:, g, at], ps[:, bank, at], TINY, None, ALU.max).then_inc(sums_safe, 1)
                dve.wait_ge(sums_safe, step + 1)
                nc.vector.reciprocal(recip[:, g, at], sums[:, g, at]).then_inc(recip_ready, 1)
                dve.wait_ge(recip_ready, step + 1)
                nc.vector.tensor_copy(
                    recip_rows[:, g, first * P:(first + tiles) * P].rearrange("p (j c) -> p j c", c=CT),
                    recip[:, g, at].rearrange("p (j c) -> p j c", c=1).to_broadcast([P, tiles * HG, CT]),
                ).then_inc(recip_repeated, 1)

            def normalise(step, bank, g, first, tiles):
                at = slice(first * P, (first + tiles) * P)
                dve.wait_ge(recip_spread, step + 1)
                nc.vector.tensor_tensor(ctxT[:, g, at], ps[:, bank, at], U[:, g, at], ALU.mult).then_inc(ctx_ready, 1)

            invert_sums(0, MISC_BANK, 0, 0, BT)
            normalise(0, MISC_BANK, 0, 0, BT)
            dve.wait_ge(out_projected, 1)
            dve.wait_ge(resid_ready, 1)
            nc.vector.tensor_tensor(partial[:, :, :], ps[:, MISC_BANK, :].rearrange("p (t c) -> p t c", t=BT),
                                    resid[:, :, :], ALU.add).then_inc(partial_ready, 1)
            for i in range(HALVES):
                invert_sums(1 + i, TAIL_SUMS[i], 1, i * HT_TILES, HT_TILES)
            for i in range(HALVES):
                normalise(1 + i, TAIL_SPREAD[i], 1, i * HT_TILES, HT_TILES)
            dve.wait_ge(partial_ready, 1)
            for i in range(HALVES):
                tiles = slice(i * HT_TILES, (i + 1) * HT_TILES)
                dve.wait_ge(out_projected, 2 + i)
                nc.vector.tensor_tensor(y[:, tiles, :],
                                        ps[:, TAIL_OUT[i], :].rearrange("p (t c) -> p t c", t=BT)[:, tiles, :],
                                        partial[:, tiles, :], ALU.add).then_inc(y_ready, 1)

        @block.tensor
        def _(pe):
            pe.wait_ge(warm_set, 1)
            pe.wait_ge(idents_ready, 1)
            for _ in range(WARM_UP):
                nc.tensor.matmul(ps[:, WARM_BANK, :], ident16[:, :], warm_up[:, :], start=True, stop=True)
            pe.wait_ge(idents_ready, 3)

            def take_away(name, bank, place, n):
                pe.wait_ge(part_ready[name], n + 1)
                nc.tensor.matmul(ps[:, bank, :], minus16[:, :], parts[name][:, place, :], start=False,
                                 stop=n == PARTS - 2, skip_group_check=True).then_inc(part_taken[name], 1)

            def pick_heads(name, places, h, n):
                last = nc.tensor.matmul(ps[0:PAIR_ROWS, PICK_BANKS[name][h], :], pick[name][:, n, h, :],
                                        parts[name][:, places[n], :], start=n == 0, stop=n == PARTS - 1)
                if n == PARTS - 1:
                    last.then_inc(picked[name], 1)

            pe.wait_ge(msg_ready, 1)
            nc.tensor.matmul(ps[:, K_BANK, :], wkT, msgT[:, :], start=True, stop=False,
                             skip_group_check=True).then_inc(projected["k"], 1)
            take_away("k", K_BANK, K_PLACES[0], 0)
            for t in range(BT):
                pe.wait_ge(xn_ready, t + 1)
                last = nc.tensor.transpose(ps[:, HT_BANK, t * P:(t + 1) * P], xn[:, t, :], ident[:, :])
            last.then_inc(xT_ready, 1)
            take_away("k", K_BANK, K_PLACES[1], 1)
            pe.wait_ge(pw_loaded, 16)
            pe.wait_ge(hT_ready, 1)
            nc.tensor.matmul(ps[:, Q_BANK, :], wqT, hT[:, :], start=True, stop=False,
                             skip_group_check=True).then_inc(projected["q"], 1)
            pe.wait_ge(picks_set, 1)
            pe.wait_ge(part_ready["k"], PARTS)
            for n in range(PARTS):
                pick_heads("k", K_PLACES, 0, n)
            take_away("q", Q_BANK, Q_PLACES[0], 0)
            for n in range(PARTS):
                pick_heads("k", K_PLACES, 1, n)
            take_away("q", Q_BANK, Q_PLACES[1], 1)
            pe.wait_ge(pick_placed["k"], 1)
            for n in range(PARTS):
                pe.wait_ge(part_ready["q"], n + 1)
                for h in range(PICKED):
                    pick_heads("q", Q_PLACES, h, n)
            for t in range(NT):
                last = nc.tensor.matmul(ps[:, V_BANK, t * D:(t + 1) * D], msgT[:, t * P:(t + 1) * P], wvT,
                                        start=True, stop=True)
            last.then_inc(v_projected, 1)

            def score_by_target(h, t):
                k = h * BT + t
                if k >= len(A_BANKS):
                    pe.wait_ge(max_found, k + 1 - len(A_BANKS))
                nc.tensor.matmul(ps[:, A_BANKS[k % len(A_BANKS)], :], QS[0:PAIR_ROWS, h, t * P:(t + 1) * P],
                                 KS[0:PAIR_ROWS, h, :], start=True, stop=True).then_inc(scores_b, 1)

            def turn_max(h):
                pe.wait_ge(max_split, h + 1)
                if h >= 1:
                    pe.wait_ge(max_placed, h)
                for t in range(BT):
                    last = nc.tensor.matmul(ps[PAIR_ROWS:STACK, MAX_BANK, t * P:(t + 1) * P], neg_max[:, h, t, :],
                                            ident16[:, :], start=True, stop=True)
                last.then_inc(max_turned, 1)

            def score_by_neighbour(h, t):
                k = h * NT + t
                bank = ps[:, B_BANKS[k % len(B_BANKS)], :]
                if k >= len(B_BANKS):
                    pe.wait_ge(exp_done, k + 1 - len(B_BANKS))
                nc.tensor.matmul(bank, ident16[:, :], mask_n[:, t, :], start=True, stop=False)
                if t == 0:
                    pe.wait_ge(max_placed, h + 1)
                nc.tensor.matmul(bank, KS[0:STACK, h, t * P:(t + 1) * P], QS[0:STACK, h, :], start=False,
                                 stop=True).then_inc(scores_n, 1)

            def first_product_with_v(t):
                pe.wait_ge(exp_done, (HG - 1) * NT + t + 1)
                for j in range(HG):
                    last = nc.tensor.matmul(ps[j * CT:(j + 1) * CT, ACC_BANK, :], V[:, t, j, :], prob[:, j, t, :],
                                            start=t == 0, stop=t == NT - 1, tile_position=(0, j * CT))
                if t == NT - 1:
                    last.then_inc(pv_done, 1)

            def last_product_with_v(t):
                pe.wait_ge(exp_done, (H - 1) * NT + t + 1)
                for i in range(HALVES):
                    for j in range(HG):
                        last = nc.tensor.matmul(ps[j * CT:(j + 1) * CT, TAIL_ACC[i], 0:HB], V[:, t, HG + j, :],
                                                prob[:, HG + j, t, i * HB:(i + 1) * HB], start=t == 0,
                                                stop=t == NT - 1, tile_position=(0, j * CT))
                    if t == NT - 1:
                        last.then_inc(pv_done, 1)

            def turn_sums(step, bank, g, first, tiles):
                pe.wait_ge(u_ready, step + 1)
                for t in range(first, first + tiles):
                    last = nc.tensor.matmul(ps[:, bank, t * HG:(t + 1) * HG], U[:, g, t * P:(t + 1) * P],
                                            pick_sum[:, :], start=True, stop=True)
                last.then_inc(sums_turned, 1)

            def spread_recip(step, bank, g, first, tiles):
                pe.wait_ge(recip_repeated, step + 1)
                for t in range(first, first + tiles):
                    last = nc.tensor.matmul(ps[:, bank, t * P:(t + 1) * P], recip_rows[:, g, t * P:(t + 1) * P],
                                            ident[:, :], start=True, stop=True)
                last.then_inc(recip_spread, 1)

            def project_out(step, bank, g, first, tiles):
                pe.wait_ge(ctx_ready, step + 1)
                for t in range(first, first + tiles):
                    last = nc.tensor.matmul(ps[:, bank, t * D:(t + 1) * D], ctxT[:, g, t * P:(t + 1) * P],
                                            pw[:, (2 + g) * D:(3 + g) * D], start=True, stop=True)
                last.then_inc(out_projected, 1)

            pe.wait_ge(pick_placed["k"], PICKED)
            pe.wait_ge(pick_placed["q"], PICKED)
            pe.wait_ge(part_ready["k"], PARTS)
            for k in range(A_AHEAD):
                score_by_target(k // BT, k % BT)
                if k == BT:
                    turn_max(0)
            pe.wait_ge(mask_n_ready, 1)
            pe.wait_ge(ones_ready, 2)
            pe.wait_ge(v_ready, 1)
            pe.wait_ge(pick_ready, 1)
            for k in range(H * NT):
                if k + A_AHEAD == PICKED * BT:
                    pe.wait_ge(stacked["k"], 16 * len(SLOT_RUNS))
                    pe.wait_ge(stacked["q"], 16 * len(SLOT_RUNS))
                if k + A_AHEAD < H * BT:
                    score_by_target((k + A_AHEAD) // BT, (k + A_AHEAD) % BT)
                score_by_neighbour(k // NT, k % NT)
                if k % NT == 2 and k // NT + 1 < H:
                    turn_max(k // NT + 1)
                if k - PV_AT in range(0, 2 * NT, 2):
                    first_product_with_v((k - PV_AT) // 2)
                if k == PV_AT + 2 * NT:
                    turn_sums(0, MISC_BANK, 0, 0, BT)
                if k == PV_AT + 2 * NT + 2:
                    spread_recip(0, MISC_BANK, 0, 0, BT)
                if k == PV_AT + 2 * NT + 4:
                    project_out(0, MISC_BANK, 0, 0, BT)
            pe.wait_ge(u_ready, 1)
            pe.wait_ge(max_found, H * BT)
            for t in range(NT):
                last_product_with_v(t)
            pe.wait_ge(max_placed, H)
            pe.wait_ge(partial_ready, 1)
            pe.wait_ge(exp_done, H * NT)
            for i in range(HALVES):
                turn_sums(1 + i, TAIL_SUMS[i], 1, i * HT_TILES, HT_TILES)
            for i in range(HALVES):
                spread_recip(1 + i, TAIL_SPREAD[i], 1, i * HT_TILES, HT_TILES)
            for i in range(HALVES):
                project_out(1 + i, TAIL_OUT[i], 1, i * HT_TILES, HT_TILES)


def kernel(x, adj, L0_gnn_h_neigh, L0_gnn_Wq, L0_gnn_bq, L0_gnn_Wk, L0_gnn_bk, L0_gnn_Wv, L0_gnn_bv, L0_gnn_Wo,
           L0_gnn_bo, L0_gnn_E):
    import numpy as np
    import concourse.bacc as bacc
    from concourse.bass_utils import run_bass_kernel_spmd

    x, adj, hn = np.asarray(x), np.asarray(adj), np.asarray(L0_gnn_h_neigh)
    Wq, Wk, Wv, Wo = (np.asarray(w) for w in (L0_gnn_Wq, L0_gnn_Wk, L0_gnn_Wv, L0_gnn_Wo))
    bq, bk, bv, bo = (np.asarray(b) for b in (L0_gnn_bq, L0_gnn_bk, L0_gnn_bv, L0_gnn_bo))
    E = np.asarray(L0_gnn_E)

    def by_dim(w):
        return w.reshape(H, DH, -1).transpose(1, 0, 2).reshape(D, -1)

    wo = np.zeros((G, HG, CT, D), Wo.dtype)
    wo[:, :, :DH] = Wo.T.reshape(G, HG, DH, D)
    cols = [by_dim(bq), by_dim(bk), E[1][:, None], np.zeros((D, 1), E.dtype)]
    arrays = {
        "x_dram": x.reshape(P, BT * D),
        "adj_b_dram": adj.reshape(P, BT * N),
        "adj_n_dram": adj.reshape(P, BT, NT, P).transpose(3, 2, 1, 0).reshape(P, NT * B),
        "pack_k_dram": np.concatenate([hn.T, by_dim(Wk).T, *cols], axis=1),
        "pack_w_dram": np.concatenate([by_dim(Wq).T, Wv.T, *wo.reshape(G, P, D)], axis=1),
        "bias_rows_dram": np.concatenate([bv, bo])[None],
    }
    arrays = {n: np.ascontiguousarray(a) for n, a in arrays.items()}
    nc = bacc.Bacc("TRN2", target_bir_lowering=False, num_devices=1)
    args = [nc.dram_tensor(n, a.shape, mybir.dt.from_np(a.dtype), kind="ExternalInput").ap() for n, a in arrays.items()]
    out = nc.dram_tensor("out_dram", (P, BT * D), mybir.dt.float32, kind="ExternalOutput").ap()
    gnn_kernel(nc, *args, out)
    r = run_bass_kernel_spmd(nc, [arrays], core_ids=[0])
    return r.results[0]["out_dram"].reshape(B, D)
```

```python
from contextlib import ExitStack

import concourse.bass as bass
from concourse import mybir

B, N, D, H = 512, 512, 128, 8
DH = D // H
P = 128
BT, NT = B // P, N // P
PARTS = 3
Q_SLOTS = (0, 1, 2, 0, 1, 0)
K_SLOTS = (2, 1, 0, 1, 0, 0)
Q_PLACES = (0, 1, 2)
K_PLACES = (2, 1, 0)
SLOT_RUNS = ((0, 3), (3, 2), (5, 1))
PICKED = 2
PAIR_ROWS = DH * len(Q_SLOTS)
MAX_ROWS = 2
STACK = PAIR_ROWS + MAX_ROWS
G = 2
HG = H // G
CT = P // HG
MASKED = -(2.0**30)
FLOOR = -(2.0**29)
TINY = 1e-30
EPS = 1e-5
A_BANKS = (0, 1, 7)
A_AHEAD = 8
B_BANKS = (2, 3, 4)
ACC_BANK, MAX_BANK, MISC_BANK = 5, 6, 7
PV_AT = H * NT - A_AHEAD
K_BANKS, Q_BANKS, HT_BANK, WARM_BANK, V_BANK = (0, 1), (2, 5), 3, 6, 7
PICK_BANKS = {"k": (4, 6), "q": (1, 3)}
POOL_TILE = 2
PIECES = ((0, 2), (2, BT - 2))
HALVES = 2
HB = B // HALVES
TAIL_ACC, TAIL_SUMS, TAIL_SPREAD, TAIL_OUT = (5, 0), (7, 6), (1, 2), (3, 4)
WARM_UP = 9
KEEP_WARM = 1
DVE_MASKED = H * NT - A_AHEAD


def gnn_kernel(nc, x_in, adj_b, adj_n, pack_k, pack_w, bias_rows, out):
    f32, bf16, i32 = mybir.dt.float32, mybir.dt.bfloat16, mybir.dt.int32
    ACT = mybir.ActivationFunctionType
    ALU = mybir.AluOpType

    ctx = ExitStack()
    with ctx:
        def sb(name, shape, dt=f32):
            return ctx.enter_context(nc.sbuf_tensor(name, shape, dt))

        def sem(name):
            return ctx.enter_context(nc.semaphore(name))

        part_dram = {
            "q": nc.dram_tensor("q_parts_dram", (PARTS, D, B), bf16, kind="Internal").ap(),
            "k": nc.dram_tensor("k_parts_dram", (PARTS, D, N), bf16, kind="Internal").ap(),
        }

        xt = sb("xt", [P, BT, D])
        xn = sb("xn", [P, BT, D])
        stats = sb("stats", [P, BT, 6])
        mean_var = sb("mean_var", [P, BT, 2])
        std = sb("std", [P, BT])
        rstd = sb("rstd", [P, BT])
        eps = sb("eps", [P, 1])
        warm = sb("warm", [P, 1])
        warm2 = sb("warm2", [P, 1])
        hT = sb("hT", [P, B])
        pk = sb("pk", [P, N + D + 4])
        hnT, wkT = pk[:, 0:N], pk[:, N:N + D]
        bq_col, bk_col, e1_col = (pk[:, N + D + i:N + D + i + 1] for i in range(3))
        pw = sb("pw", [P, 4 * D])
        wqT, wvT = pw[:, 0:D], pw[:, D:2 * D]
        brow = sb("brow", [P, 2 * D])
        bv_row, bo_row = brow[:, 0:D], brow[:, D:2 * D]
        msgT = sb("msgT", [P, N])
        parts = {"q": sb("q_parts", [P, PARTS, B], bf16), "k": sb("k_parts", [P, PARTS, N], bf16)}
        QS = sb("QS", [P, H, B], bf16)
        KS = sb("KS", [P, H, N], bf16)
        adj_b_sb = sb("adj_b_sb", [P, BT * N], i32)
        adj_n_sb = sb("adj_n_sb", [P, NT * B], i32)
        mask_b = sb("mask_b", [P, BT, N], bf16)
        mask_n = sb("mask_n", [P, NT, B], bf16)
        V = sb("V", [P, NT, H, CT])
        masked_scores = sb("masked_scores", [P, len(A_BANKS), N], bf16)
        masked_n = sb("masked_n", [P, H * NT - DVE_MASKED, B])
        row_max = sb("row_max", [P, H, BT])
        max_parts = sb("max_parts", [P, H, BT, MAX_ROWS], bf16)
        prob = sb("prob", [P, H, NT, B])
        ident = sb("ident", [P, P])
        ident16 = sb("ident16", [P, P], bf16)
        minus16 = sb("minus16", [P, P], bf16)
        warm_up = sb("warm_up", [P, 512], bf16)
        pick = {"q": sb("q_pick", [P, PARTS, PICKED, PAIR_ROWS], bf16),
                "k": sb("k_pick", [P, PARTS, PICKED, PAIR_ROWS], bf16)}
        pick_sum = sb("pick_sum", [P, HG])
        U = sb("U", [P, G, B])
        recip = sb("recip", [P, G, BT * HG])
        tiny = sb("tiny", [P, 1])
        ctxT = sb("ctxT", [P, G, B])
        resid = sb("resid", [P, BT, D])
        y = sb("y", [P, BT, D])
        ps = ctx.enter_context(nc.psum_tensor("ps", [P, 8, 512], f32))

        x_loaded, pk_loaded, pw_loaded, rows_loaded = (
            sem("x_loaded"), sem("pk_loaded"), sem("pw_loaded"), sem("rows_loaded"))
        adj_b_loaded, adj_n_loaded = sem("adj_b_loaded"), sem("adj_n_loaded")
        part_written = {"q": sem("q_part_written"), "k": sem("k_part_written")}
        stacked = {"q": sem("q_stacked"), "k": sem("k_stacked")}
        stored = [sem(f"stored{i}") for i in range(HALVES)]
        eps_set, idents_zero, idents_ready, pick_ready, ones_ready = (
            sem("eps_set"), sem("idents_zero"), sem("idents_ready"), sem("pick_ready"), sem("ones_ready"))
        msg_ready, stats_ready, mean_ready, std_ready, rstd_ready, xn_ready = (
            sem("msg_ready"), sem("stats_ready"), sem("mean_ready"), sem("std_ready"), sem("rstd_ready"),
            sem("xn_ready"))
        xT_ready, hT_ready = sem("xT_ready"), sem("hT_ready")
        projected = {"q": sem("q_projected"), "k": sem("k_projected")}
        part_ready = {"q": sem("q_part_ready"), "k": sem("k_part_ready")}
        part_taken = {"q": sem("q_part_taken"), "k": sem("k_part_taken")}
        half_ready = {"q": sem("q_half_ready"), "k": sem("k_half_ready")}
        half_taken = {"q": sem("q_half_taken"), "k": sem("k_half_taken")}
        picked = {"q": sem("q_picked"), "k": sem("k_picked")}
        pick_placed = {"q": sem("q_pick_placed"), "k": sem("k_pick_placed")}
        warm_set, picks_zero, picks_set = sem("warm_set"), sem("picks_zero"), sem("picks_set")
        v_projected, v_ready = sem("v_projected"), sem("v_ready")
        mask_b_ready, mask_n_ready, mask_b_pool_ready, mask_n_pool_ready = (
            sem("mask_b_ready"), sem("mask_n_ready"), sem("mask_b_pool_ready"), sem("mask_n_pool_ready"))
        masked_ready = sem("masked_ready")
        scores_b, max_found, high_ready, max_split, max_turned, max_placed = (
            sem("scores_b"), sem("max_found"), sem("high_ready"), sem("max_split"), sem("max_turned"),
            sem("max_placed"))
        scores_n, exp_done, pv_done, u_ready = sem("scores_n"), sem("exp_done"), sem("pv_done"), sem("u_ready")
        sums_turned, tiny_ready, recip_ready, recip_spread, ctx_ready = (
            sem("sums_turned"), sem("tiny_ready"), sem("recip_ready"), sem("recip_spread"), sem("ctx_ready"))
        out_projected, resid_ready, y_ready = sem("out_projected"), sem("resid_ready"), sem("y_ready")

        block = ctx.enter_context(nc.Block())

        @block.sync
        def _(sp):
            sp.dma_start(xt[:, :, :], x_in).then_inc(x_loaded, 16)
            sp.dma_start(pw[:, :], pack_w).then_inc(pw_loaded, 16)
            for name in ("k", "q"):
                sp.wait_ge(part_ready[name], PARTS)
                sp.wait_ge(half_ready[name], PARTS)
                sp.dma_start(part_dram[name].rearrange("s f b -> f s b"), parts[name][:, :, :]).then_inc(
                    part_written[name], 16)
            for name, stack, slots, places in (("k", KS, K_SLOTS, K_PLACES), ("q", QS, Q_SLOTS, Q_PLACES)):
                sp.wait_ge(part_written[name], 16)
                rows = part_dram[name].rearrange("s (d h) b -> (s d) h b", h=H)
                for slot, length in SLOT_RUNS:
                    place = places[slots[slot]]
                    sp.dma_start(stack[DH * slot:DH * (slot + length), PICKED:H, :],
                                 rows[DH * place:DH * (place + length), PICKED:H, :]).then_inc(stacked[name], 16)
            sp.wait_ge(y_ready, 1)
            sp.dma_start(out[:, 0:PIECES[0][1] * D], y[:, 0:PIECES[0][1], :]).then_inc(stored[0], 16)
            sp.wait_ge(stored[0], 16)

        @block.gpsimd
        def _(pool):
            nc.gpsimd.memset(eps[:, :], EPS).then_inc(eps_set, 1)
            nc.gpsimd.memset(ident[:, :], 0.0)
            nc.gpsimd.memset(ident16[:, :], 0.0)
            nc.gpsimd.memset(minus16[:, :], 0.0)
            nc.gpsimd.memset(pick_sum[:, :], 0.0).then_inc(idents_zero, 1)
            pool.wait_ge(idents_zero, 1)
            for m, value in ((ident16, 1.0), (ident, 1.0), (minus16, -1.0)):
                nc.gpsimd.affine_select(out=m[:, :], in_=m[:, :], compare_op=ALU.not_equal, fill=value, base=0,
                                        pattern=[[-1, P]], channel_multiplier=1).then_inc(idents_ready, 1)
            nc.gpsimd.affine_select(out=pick_sum[:, :], in_=pick_sum[:, :], compare_op=ALU.not_equal, fill=1.0,
                                    base=-DH, pattern=[[-CT, HG]], channel_multiplier=1).then_inc(pick_ready, 1)
            nc.gpsimd.memset(V[:, :, :, :], 1.0).then_inc(ones_ready, 1)
            nc.gpsimd.memset(tiny[:, :], TINY).then_inc(tiny_ready, 1)
            pool.wait_ge(tiny_ready, 1)
            for j in range(HG):
                nc.gpsimd.memset(tiny[j * CT:j * CT + DH, :], 0.0).then_inc(tiny_ready, 1)
            pool.wait_ge(ones_ready, 1)
            nc.gpsimd.memset(KS[PAIR_ROWS:STACK, :, :], 1.0).then_inc(ones_ready, 1)
            pool.wait_ge(ones_ready, 2)
            pool.wait_ge(x_loaded, 16)
            pool.wait_ge(rows_loaded, 16)
            nc.gpsimd.tensor_tensor(resid[:, :, :], xt[:, :, :],
                                    bo_row.rearrange("p (t c) -> p t c", t=1).to_broadcast([P, BT, D]),
                                    ALU.add).then_inc(resid_ready, 1)
            pool.wait_ge(adj_b_loaded, 16)
            pool.wait_ge(resid_ready, 1)
            for t in range(POOL_TILE, BT):
                nc.gpsimd.tensor_scalar(mask_b[:, t, :], adj_b_sb[:, t * N:(t + 1) * N], 0.0, MASKED,
                                        ALU.is_equal, ALU.mult).then_inc(mask_b_pool_ready, 1)
            pool.wait_ge(adj_n_loaded, 16)
            for t in range(POOL_TILE, NT):
                nc.gpsimd.tensor_scalar(mask_n[:, t, :], adj_n_sb[:, t * B:(t + 1) * B], 0.0, MASKED,
                                        ALU.is_equal, ALU.mult).then_inc(mask_n_pool_ready, 1)
            for h in range(H):
                pool.wait_ge(max_found, (h + 1) * BT)
                nc.gpsimd.tensor_copy(max_parts[:, h, :, 0], row_max[:, h, :]).then_inc(high_ready, 1)
                pool.wait_ge(high_ready, h + 1)
                nc.gpsimd.tensor_tensor(max_parts[:, h, :, 1], row_max[:, h, :], max_parts[:, h, :, 0],
                                        ALU.subtract).then_inc(max_split, 1)

        @block.scalar
        def _(act):
            act.dma_start(pk[:, :], pack_k).then_inc(pk_loaded, 16)
            act.dma_start(brow[:, :], bias_rows.to_broadcast([P, 2 * D])).then_inc(rows_loaded, 16)
            act.dma_start(adj_b_sb[:, :], adj_b).then_inc(adj_b_loaded, 16)
            act.dma_start(adj_n_sb[:, :], adj_n).then_inc(adj_n_loaded, 16)
            act.wait_ge(eps_set, 1)
            nc.scalar.activation(warm[:, :], eps[:, :], ACT.Sqrt)

            def take_part(name, bank, bias, place, n):
                if n == 0:
                    act.wait_ge(projected[name], 1)
                else:
                    act.wait_ge(part_taken[name], n)
                nc.scalar.activation(parts[name][:, place, 0:HB], ps[:, bank, 0:HB], ACT.Identity,
                                     bias=bias).then_inc(part_ready[name], 1)

            def place_stack(name, stack, h):
                act.wait_ge(picked[name], h + 1)
                nc.scalar.activation(stack[0:PAIR_ROWS, h, :], ps[0:PAIR_ROWS, PICK_BANKS[name][h], :],
                                     ACT.Copy).then_inc(pick_placed[name], 1)

            act.wait_ge(mean_ready, 1)
            nc.scalar.activation(std[:, :], mean_var[:, :, 1], ACT.Sqrt, bias=eps[:, :]).then_inc(std_ready, 1)
            for n in range(PARTS):
                take_part("k", K_BANKS[0], bk_col, K_PLACES[n], n)
            for n in range(PARTS):
                take_part("q", Q_BANKS[0], bq_col, Q_PLACES[n], n)
                if n == 0:
                    place_stack("k", KS, 0)
            place_stack("q", QS, 0)
            place_stack("q", QS, 1)
            nc.scalar.activation(warm2[:, :], eps[:, :], ACT.Exp)

            def place_max(h):
                act.wait_ge(max_turned, h + 1)
                nc.scalar.activation(QS[PAIR_ROWS:STACK, h, :], ps[PAIR_ROWS:STACK, MAX_BANK, :],
                                     ACT.Copy).then_inc(max_placed, 1)

            place_max(0)
            for h in range(H):
                for t in range(NT):
                    k = h * NT + t
                    if k == PV_AT + NT - 1:
                        act.wait_ge(pv_done, 1)
                        act.wait_ge(tiny_ready, 1 + HG)
                        nc.scalar.activation(U[:, 0, :], ps[:, ACC_BANK, :], ACT.Identity,
                                             bias=tiny[:, :]).then_inc(u_ready, 1)
                    if k < DVE_MASKED:
                        act.wait_ge(scores_n, k + 1)
                        scores = ps[:, B_BANKS[k % len(B_BANKS)], :]
                    else:
                        act.wait_ge(masked_ready, k + 1 - DVE_MASKED)
                        scores = masked_n[:, k - DVE_MASKED, :]
                    nc.scalar.activation(prob[:, h, t, :], scores, ACT.Exp, scale=DH ** -0.5).then_inc(exp_done, 1)
                    if t == 1 and h + 1 < H:
                        place_max(h + 1)
            for i, (first, tiles) in enumerate(PIECES):
                act.wait_ge(pv_done, 2 + i)
                nc.scalar.activation(U[:, 1, first * P:(first + tiles) * P], ps[:, TAIL_ACC[i], 0:tiles * P],
                                     ACT.Identity, bias=tiny[:, :]).then_inc(u_ready, 1)
            act.wait_ge(y_ready, 2)
            act.dma_start(out[:, PIECES[1][0] * D:BT * D], y[:, PIECES[1][0]:BT, :]).then_inc(stored[1], 16)
            act.wait_ge(stored[1], 16)

        @block.vector
        def _(dve):
            nc.vector.memset(warm_up[:, :], 1.0).then_inc(warm_set, 1)
            nc.vector.memset(pick["q"][:, :, :, :], 0.0).then_inc(picks_zero, 1)
            nc.vector.memset(pick["k"][:, :, :, :], 0.0).then_inc(picks_zero, 1)
            dve.wait_ge(picks_zero, 2)
            dve.wait_ge(idents_ready, 1)
            by_head = ident16[:, :].rearrange("p (d h) -> p h d", h=H)
            for name, slots in (("q", Q_SLOTS), ("k", K_SLOTS)):
                for slot in range(len(slots)):
                    last = nc.vector.tensor_copy(
                        pick[name][:, slots[slot], :, DH * slot:DH * (slot + 1)], by_head[:, 0:PICKED, :])
            last.then_inc(picks_set, 1)
            dve.wait_ge(x_loaded, 16)
            for t in range(BT):
                last = nc.vector.bn_stats(stats[:, t, :], xt[:, t, :])
            last.then_inc(stats_ready, 1)
            dve.wait_ge(stats_ready, 1)
            for t in range(BT):
                last = nc.vector.bn_aggr(mean_var[:, t, :], stats[:, t, :])
            last.then_inc(mean_ready, 1)
            dve.wait_ge(pk_loaded, 16)
            nc.vector.tensor_scalar(msgT[:, :], hnT, e1_col, None, ALU.add).then_inc(msg_ready, 1)
            dve.wait_ge(std_ready, 1)
            nc.vector.reciprocal(rstd[:, :], std[:, :]).then_inc(rstd_ready, 1)
            dve.wait_ge(mean_ready, 1)
            dve.wait_ge(rstd_ready, 1)
            for t in range(BT):
                nc.vector.tensor_scalar(xn[:, t, :], xt[:, t, :], mean_var[:, t, 0:1], rstd[:, t:t + 1],
                                        ALU.subtract, ALU.mult).then_inc(xn_ready, 1)

            def take_part(name, bank, bias, place, n):
                if n == 0:
                    dve.wait_ge(projected[name], 2)
                else:
                    dve.wait_ge(half_taken[name], n)
                nc.vector.tensor_scalar(parts[name][:, place, HB:B], ps[:, bank, 0:HB], bias, None,
                                        ALU.add).then_inc(half_ready[name], 1)

            def place_v(t):
                nc.vector.tensor_tensor(
                    V[:, t, :, 0:DH], ps[:, V_BANK, t * D:(t + 1) * D].rearrange("p (h d) -> p h d", h=H),
                    bv_row.rearrange("p (h d) -> p h d", h=H), ALU.add).then_inc(v_ready, 1)

            take_part("k", K_BANKS[1], bk_col, K_PLACES[0], 0)
            dve.wait_ge(xT_ready, 1)
            nc.vector.tensor_scalar(hT[:, :], ps[:, HT_BANK, :], 0.0, None, ALU.max).then_inc(hT_ready, 1)
            take_part("k", K_BANKS[1], bk_col, K_PLACES[1], 1)
            dve.wait_ge(adj_b_loaded, 16)
            nc.vector.tensor_scalar(mask_b[:, 0:POOL_TILE, :],
                                    adj_b_sb[:, 0:POOL_TILE * N].rearrange("p (t n) -> p t n", n=N), 0.0, MASKED,
                                    ALU.is_equal, ALU.mult).then_inc(mask_b_ready, 1)
            take_part("k", K_BANKS[1], bk_col, K_PLACES[2], 2)
            dve.wait_ge(v_projected, 2)
            dve.wait_ge(ones_ready, 1)
            dve.wait_ge(rows_loaded, 16)
            for n in range(PARTS):
                take_part("q", Q_BANKS[1], bq_col, Q_PLACES[n], n)
                place_v(n)
            place_v(NT - 1)
            dve.wait_ge(picked["k"], PICKED)
            nc.vector.tensor_copy(KS[0:PAIR_ROWS, 1, :], ps[0:PAIR_ROWS, PICK_BANKS["k"][1], :]).then_inc(
                pick_placed["k"], 1)
            dve.wait_ge(adj_n_loaded, 16)
            nc.vector.tensor_scalar(mask_n[:, 0:POOL_TILE, :],
                                    adj_n_sb[:, 0:POOL_TILE * B].rearrange("p (t b) -> p t b", b=B), 0.0,
                                    MASKED, ALU.is_equal, ALU.mult).then_inc(mask_n_ready, 1)

            dve.wait_ge(mask_b_ready, 1)
            for h in range(H):
                for t in range(BT):
                    k = h * BT + t
                    if h == 0 and t >= POOL_TILE:
                        dve.wait_ge(mask_b_pool_ready, t + 1 - POOL_TILE)
                    dve.wait_ge(scores_b, k + 1)
                    nc.vector.tensor_tensor_reduce(
                        out=masked_scores[:, k % len(A_BANKS), :], in0=ps[:, A_BANKS[k % len(A_BANKS)], :], in1=mask_b[:, t, :],
                        scale=1.0, scalar=FLOOR, op0=ALU.add, op1=ALU.max,
                        accum_out=row_max[:, h, t:t + 1]).then_inc(max_found, 1)

            def invert_sums(step, bank, g, first, tiles):
                at = slice(first * HG, (first + tiles) * HG)
                dve.wait_ge(sums_turned, step + 1)
                nc.vector.reciprocal(recip[:, g, at], ps[:, bank, at]).then_inc(recip_ready, 1)

            def normalise(step, bank, g, first, tiles):
                at = slice(first * P, (first + tiles) * P)
                dve.wait_ge(recip_spread, step + 1)
                nc.vector.tensor_tensor(ctxT[:, g, at], ps[:, bank, at], U[:, g, at], ALU.mult).then_inc(ctx_ready, 1)

            def mask_scores(k):
                dve.wait_ge(scores_n, k + 1)
                nc.vector.tensor_tensor(masked_n[:, k - DVE_MASKED, :], ps[:, B_BANKS[k % len(B_BANKS)], :],
                                        mask_n[:, k % NT, :], ALU.add).then_inc(masked_ready, 1)

            for k in range(DVE_MASKED, H * NT - 1):
                mask_scores(k)
            invert_sums(0, MISC_BANK, 0, 0, BT)
            mask_scores(H * NT - 1)
            normalise(0, MISC_BANK, 0, 0, BT)
            invert_sums(1, TAIL_SUMS[0], 1, *PIECES[0])
            def finish(i):
                tiles = slice(PIECES[i][0], sum(PIECES[i]))
                dve.wait_ge(resid_ready, 1)
                dve.wait_ge(out_projected, 1 + i)
                nc.vector.tensor_tensor(y[:, tiles, :],
                                        ps[:, TAIL_OUT[i], :].rearrange("p (t c) -> p t c", t=BT)[:, tiles, :],
                                        resid[:, tiles, :], ALU.add).then_inc(y_ready, 1)

            normalise(1, TAIL_SPREAD[0], 1, *PIECES[0])
            invert_sums(2, TAIL_SUMS[1], 1, *PIECES[1])
            normalise(2, TAIL_SPREAD[1], 1, *PIECES[1])
            finish(0)
            finish(1)

        @block.tensor
        def _(pe):
            pe.wait_ge(warm_set, 1)
            for _ in range(WARM_UP):
                nc.tensor.matmul(ps[:, WARM_BANK, :], warm_up[:, 0:P], warm_up[:, :], start=True, stop=True)
            pe.wait_ge(idents_ready, 3)

            def take_away(name, banks, place, n):
                for i, ready, taken in ((0, part_ready, part_taken), (1, half_ready, half_taken)):
                    pe.wait_ge(ready[name], n + 1)
                    nc.tensor.matmul(ps[:, banks[i], 0:HB], minus16[:, :],
                                     parts[name][:, place, i * HB:(i + 1) * HB], start=False, stop=n == PARTS - 2,
                                     skip_group_check=True).then_inc(taken[name], 1)

            def project(name, banks, weights, operand):
                for i in range(HALVES):
                    nc.tensor.matmul(ps[:, banks[i], 0:HB], weights, operand[:, i * HB:(i + 1) * HB], start=True,
                                     stop=False, skip_group_check=True).then_inc(projected[name], 1)

            def pick_heads(name, places, h, n):
                last = nc.tensor.matmul(ps[0:PAIR_ROWS, PICK_BANKS[name][h], :], pick[name][:, n, h, :],
                                        parts[name][:, places[n], :], start=n == 0, stop=n == PARTS - 1)
                if n == PARTS - 1:
                    last.then_inc(picked[name], 1)

            pe.wait_ge(msg_ready, 1)
            project("k", K_BANKS, wkT, msgT)
            for t in range(BT):
                pe.wait_ge(xn_ready, t + 1)
                last = nc.tensor.transpose(ps[:, HT_BANK, t * P:(t + 1) * P], xn[:, t, :], ident[:, :])
            last.then_inc(xT_ready, 1)
            pe.wait_ge(pw_loaded, 16)

            def project_v(tiles):
                for t in tiles:
                    last = nc.tensor.matmul(ps[:, V_BANK, t * D:(t + 1) * D], msgT[:, t * P:(t + 1) * P], wvT,
                                            start=True, stop=True)
                last.then_inc(v_projected, 1)

            project_v((0, 1))
            take_away("k", K_BANKS, K_PLACES[0], 0)
            project_v((2, 3))
            pe.wait_ge(hT_ready, 1)
            project("q", Q_BANKS, wqT, hT)
            take_away("k", K_BANKS, K_PLACES[1], 1)
            pe.wait_ge(picks_set, 1)

            pe.wait_ge(part_ready["k"], PARTS)
            pe.wait_ge(half_ready["k"], PARTS)
            for n in range(PARTS):
                pick_heads("k", K_PLACES, 0, n)
            take_away("q", Q_BANKS, Q_PLACES[0], 0)
            for n in range(PARTS):
                pick_heads("k", K_PLACES, 1, n)
            take_away("q", Q_BANKS, Q_PLACES[1], 1)
            pe.wait_ge(part_ready["q"], PARTS)
            pe.wait_ge(half_ready["q"], PARTS)
            for h in range(PICKED):
                for n in range(PARTS):
                    pick_heads("q", Q_PLACES, h, n)

            def score_by_target(h, t):
                k = h * BT + t
                if A_BANKS[k % len(A_BANKS)] == V_BANK:
                    pe.wait_ge(v_ready, NT)
                if k >= len(A_BANKS):
                    pe.wait_ge(max_found, k + 1 - len(A_BANKS))
                nc.tensor.matmul(ps[:, A_BANKS[k % len(A_BANKS)], :], QS[0:PAIR_ROWS, h, t * P:(t + 1) * P],
                                 KS[0:PAIR_ROWS, h, :], start=True, stop=True).then_inc(scores_b, 1)

            def turn_max(h):
                pe.wait_ge(max_split, h + 1)
                if h >= 1:
                    pe.wait_ge(max_placed, h)
                for t in range(BT):
                    last = nc.tensor.matmul(ps[PAIR_ROWS:STACK, MAX_BANK, t * P:(t + 1) * P], max_parts[:, h, t, :],
                                            minus16[:, :], start=True, stop=True)
                last.then_inc(max_turned, 1)

            def score_by_neighbour(h, t):
                k = h * NT + t
                bank = ps[:, B_BANKS[k % len(B_BANKS)], :]
                before = k - len(B_BANKS)
                if before >= DVE_MASKED:
                    pe.wait_ge(masked_ready, before + 1 - DVE_MASKED)
                elif before >= 0:
                    pe.wait_ge(exp_done, before + 1)
                if k < DVE_MASKED:
                    if k == 0:
                        pe.wait_ge(mask_n_ready, 1)
                    if POOL_TILE <= k < NT:
                        pe.wait_ge(mask_n_pool_ready, k + 1 - POOL_TILE)
                    nc.tensor.matmul(bank, ident16[:, :], mask_n[:, t, :], start=True, stop=False)
                if t == 0:
                    pe.wait_ge(max_placed, h + 1)
                nc.tensor.matmul(bank, KS[0:STACK, h, t * P:(t + 1) * P], QS[0:STACK, h, :], start=k >= DVE_MASKED,
                                 stop=True).then_inc(scores_n, 1)

            def first_product_with_v(t):
                pe.wait_ge(exp_done, (HG - 1) * NT + t + 1)
                for j in range(HG):
                    last = nc.tensor.matmul(ps[j * CT:(j + 1) * CT, ACC_BANK, :], V[:, t, j, :], prob[:, j, t, :],
                                            start=t == 0, stop=t == NT - 1, tile_position=(0, j * CT))
                if t == NT - 1:
                    last.then_inc(pv_done, 1)

            def last_product_with_v(i, t):
                pe.wait_ge(exp_done, (H - 1) * NT + t + 1)
                first, tiles = PIECES[i]
                for j in range(HG):
                    last = nc.tensor.matmul(ps[j * CT:(j + 1) * CT, TAIL_ACC[i], 0:tiles * P], V[:, t, HG + j, :],
                                            prob[:, HG + j, t, first * P:(first + tiles) * P], start=t == 0,
                                            stop=t == NT - 1, tile_position=(0, j * CT))
                if t == NT - 1:
                    last.then_inc(pv_done, 1)

            def turn_sums(step, bank, g, first, tiles):
                pe.wait_ge(u_ready, step + 1)
                for t in range(first, first + tiles):
                    last = nc.tensor.matmul(ps[:, bank, t * HG:(t + 1) * HG], U[:, g, t * P:(t + 1) * P],
                                            pick_sum[:, :], start=True, stop=True)
                last.then_inc(sums_turned, 1)

            def spread_recip(step, bank, g, first, tiles):
                pe.wait_ge(recip_ready, step + 1)
                for t in range(first, first + tiles):
                    for j in range(HG):
                        last = nc.tensor.matmul(
                            ps[j * CT:(j + 1) * CT, bank, t * P:(t + 1) * P],
                            recip[:, g, t * HG + j:t * HG + j + 1].to_broadcast([P, CT]), ident[:, :],
                            start=True, stop=True, tile_position=(0, j * CT))
                last.then_inc(recip_spread, 1)

            def project_out(i, g):
                pe.wait_ge(ctx_ready, 1 if g == 0 else 2 + i)
                first, tiles = PIECES[i]
                for t in range(first, first + tiles):
                    last = nc.tensor.matmul(ps[:, TAIL_OUT[i], t * D:(t + 1) * D], ctxT[:, g, t * P:(t + 1) * P],
                                            pw[:, (2 + g) * D:(3 + g) * D], start=g == 0 and t == first, stop=g == G - 1,
                                            skip_group_check=True)
                if g == G - 1:
                    last.then_inc(out_projected, 1)

            pe.wait_ge(pick_placed["k"], 1)
            pe.wait_ge(pick_placed["q"], 1)
            for k in range(A_AHEAD):
                if k == BT:
                    pe.wait_ge(pick_placed["k"], PICKED)
                    pe.wait_ge(pick_placed["q"], PICKED)
                score_by_target(k // BT, k % BT)
                if k == BT + 2:
                    turn_max(0)
                for _ in range(KEEP_WARM):
                    nc.tensor.matmul(ps[:, ACC_BANK, :], ident16[:, :], warm_up[:, :], start=True, stop=True)
            pe.wait_ge(ones_ready, 2)
            pe.wait_ge(pick_ready, 1)
            pe.wait_ge(v_ready, NT)
            for k in range((H - 1) * NT):
                if k + A_AHEAD == PICKED * BT:
                    pe.wait_ge(stacked["k"], 16 * len(SLOT_RUNS))
                    pe.wait_ge(stacked["q"], 16 * len(SLOT_RUNS))
                if k + A_AHEAD < H * BT:
                    score_by_target((k + A_AHEAD) // BT, (k + A_AHEAD) % BT)
                score_by_neighbour(k // NT, k % NT)
                if k % NT == NT - 2 and k // NT + 1 < H:
                    turn_max(k // NT + 1)
                if k >= PV_AT:
                    first_product_with_v(k - PV_AT)
            pe.wait_ge(max_found, H * BT)
            score_by_neighbour(H - 1, 0)
            score_by_neighbour(H - 1, 1)
            score_by_neighbour(H - 1, 2)
            turn_sums(0, MISC_BANK, 0, 0, BT)
            last_product_with_v(0, 0)
            score_by_neighbour(H - 1, 3)
            spread_recip(0, MISC_BANK, 0, 0, BT)
            last_product_with_v(0, 1)
            last_product_with_v(0, 2)
            last_product_with_v(0, 3)
            pe.wait_ge(max_placed, H)
            pe.wait_ge(exp_done, H * NT)
            project_out(0, 0)
            project_out(1, 0)
            last_product_with_v(1, 0)
            turn_sums(1, TAIL_SUMS[0], 1, *PIECES[0])
            last_product_with_v(1, 1)
            last_product_with_v(1, 2)
            last_product_with_v(1, 3)
            spread_recip(1, TAIL_SPREAD[0], 1, *PIECES[0])
            turn_sums(2, TAIL_SUMS[1], 1, *PIECES[1])
            spread_recip(2, TAIL_SPREAD[1], 1, *PIECES[1])
            project_out(0, 1)
            project_out(1, 1)


def kernel(x, adj, L0_gnn_h_neigh, L0_gnn_Wq, L0_gnn_bq, L0_gnn_Wk, L0_gnn_bk, L0_gnn_Wv, L0_gnn_bv, L0_gnn_Wo,
           L0_gnn_bo, L0_gnn_E):
    import numpy as np
    import concourse.bacc as bacc
    from concourse.bass_utils import run_bass_kernel_spmd

    x, adj, hn = np.asarray(x), np.asarray(adj), np.asarray(L0_gnn_h_neigh)
    Wq, Wk, Wv, Wo = (np.asarray(w) for w in (L0_gnn_Wq, L0_gnn_Wk, L0_gnn_Wv, L0_gnn_Wo))
    bq, bk, bv, bo = (np.asarray(b) for b in (L0_gnn_bq, L0_gnn_bk, L0_gnn_bv, L0_gnn_bo))
    E = np.asarray(L0_gnn_E)

    def by_dim(w):
        return w.reshape(H, DH, -1).transpose(1, 0, 2).reshape(D, -1)

    wo = np.zeros((G, HG, CT, D), Wo.dtype)
    wo[:, :, :DH] = Wo.T.reshape(G, HG, DH, D)
    cols = [by_dim(bq), by_dim(bk), E[1][:, None], np.zeros((D, 1), E.dtype)]
    arrays = {
        "x_dram": x.reshape(P, BT * D),
        "adj_b_dram": adj.reshape(P, BT * N),
        "adj_n_dram": adj.reshape(P, BT, NT, P).transpose(3, 2, 1, 0).reshape(P, NT * B),
        "pack_k_dram": np.concatenate([hn.T, by_dim(Wk).T, *cols], axis=1),
        "pack_w_dram": np.concatenate([by_dim(Wq).T, Wv.T, *wo.reshape(G, P, D)], axis=1),
        "bias_rows_dram": np.concatenate([bv, bo])[None],
    }
    arrays = {n: np.ascontiguousarray(a) for n, a in arrays.items()}
    nc = bacc.Bacc("TRN2", target_bir_lowering=False, num_devices=1)
    args = [nc.dram_tensor(n, a.shape, mybir.dt.from_np(a.dtype), kind="ExternalInput").ap() for n, a in arrays.items()]
    out = nc.dram_tensor("out_dram", (P, BT * D), mybir.dt.float32, kind="ExternalOutput").ap()
    gnn_kernel(nc, *args, out)
    r = run_bass_kernel_spmd(nc, [arrays], core_ids=[0])
    return r.results[0]["out_dram"].reshape(B, D)
```
